# Optimizing a Trainium2 kernel written in Bass

```python
import numpy as np
import jax
import jax.numpy as jnp

def _softmax(x, axis=-1):
    return jax.nn.softmax(x, axis=axis)

def _gelu(x):
    return jax.nn.gelu(x, approximate=True)

def _silu(x):
    return jax.nn.silu(x)

def _sigmoid(x):
    return jax.nn.sigmoid(x)

def _layernorm(x, axis=-1, eps=1e-05):
    m = jnp.mean(x, axis=axis, keepdims=True)
    v = jnp.var(x, axis=axis, keepdims=True)
    return (x - m) / jnp.sqrt(v + eps)

def _scatter_add(tgt, idx, src, axis=0):
    return tgt.at[idx].add(src)

def _segment_sum(src, seg, n):
    return jax.ops.segment_sum(src, seg, n)
kernel_name = 'mk_dlrm_tower_d1_rec_r8_5cd529'

def setup_inputs(seed: int=0):
    np.random.seed(seed)
    _w = jnp.asarray

    def _rec_inputs():
        import jax
        import jax.numpy as jnp
        _tk = jax.random.key(seed)
        ids = jnp.stack([jax.random.randint(jax.random.fold_in(_tk, 200 + f), (2048,), 0, v, jnp.int32) for f, v in enumerate([12500, 1250, 1250, 12500, 125000, 1250, 1250, 12500, 12500, 12500, 1000, 12500, 12500, 1000, 1250, 12500, 1250, 1000, 1250, 1000, 1250, 1000, 1250, 1000, 1000, 1250])], axis=1)
        tbl_0 = 0.05 * jax.random.normal(jax.random.fold_in(_tk, 500 + 0), (12500, 128), jnp.float32)
        tbl_1 = 0.05 * jax.random.normal(jax.random.fold_in(_tk, 500 + 1), (1250, 128), jnp.float32)
        tbl_2 = 0.05 * jax.random.normal(jax.random.fold_in(_tk, 500 + 2), (1250, 128), jnp.float32)
        tbl_3 = 0.05 * jax.random.normal(jax.random.fold_in(_tk, 500 + 3), (12500, 128), jnp.float32)
        tbl_4 = 0.05 * jax.random.normal(jax.random.fold_in(_tk, 500 + 4), (125000, 128), jnp.float32)
        tbl_5 = 0.05 * jax.random.normal(jax.random.fold_in(_tk, 500 + 5), (1250, 128), jnp.float32)
        tbl_6 = 0.05 * jax.random.normal(jax.random.fold_in(_tk, 500 + 6), (1250, 128), jnp.float32)
        tbl_7 = 0.05 * jax.random.normal(jax.random.fold_in(_tk, 500 + 7), (12500, 128), jnp.float32)
        tbl_8 = 0.05 * jax.random.normal(jax.random.fold_in(_tk, 500 + 8), (12500, 128), jnp.float32)
        tbl_9 = 0.05 * jax.random.normal(jax.random.fold_in(_tk, 500 + 9), (12500, 128), jnp.float32)
        tbl_10 = 0.05 * jax.random.normal(jax.random.fold_in(_tk, 500 + 10), (1000, 128), jnp.float32)
        tbl_11 = 0.05 * jax.random.normal(jax.random.fold_in(_tk, 500 + 11), (12500, 128), jnp.float32)
        tbl_12 = 0.05 * jax.random.normal(jax.random.fold_in(_tk, 500 + 12), (12500, 128), jnp.float32)
        tbl_13 = 0.05 * jax.random.normal(jax.random.fold_in(_tk, 500 + 13), (1000, 128), jnp.float32)
        tbl_14 = 0.05 * jax.random.normal(jax.random.fold_in(_tk, 500 + 14), (1250, 128), jnp.float32)
        tbl_15 = 0.05 * jax.random.normal(jax.random.fold_in(_tk, 500 + 15), (12500, 128), jnp.float32)
        tbl_16 = 0.05 * jax.random.normal(jax.random.fold_in(_tk, 500 + 16), (1250, 128), jnp.float32)
        tbl_17 = 0.05 * jax.random.normal(jax.random.fold_in(_tk, 500 + 17), (1000, 128), jnp.float32)
        tbl_18 = 0.05 * jax.random.normal(jax.random.fold_in(_tk, 500 + 18), (1250, 128), jnp.float32)
        tbl_19 = 0.05 * jax.random.normal(jax.random.fold_in(_tk, 500 + 19), (1000, 128), jnp.float32)
        tbl_20 = 0.05 * jax.random.normal(jax.random.fold_in(_tk, 500 + 20), (1250, 128), jnp.float32)
        tbl_21 = 0.05 * jax.random.normal(jax.random.fold_in(_tk, 500 + 21), (1000, 128), jnp.float32)
        tbl_22 = 0.05 * jax.random.normal(jax.random.fold_in(_tk, 500 + 22), (1250, 128), jnp.float32)
        tbl_23 = 0.05 * jax.random.normal(jax.random.fold_in(_tk, 500 + 23), (1000, 128), jnp.float32)
        tbl_24 = 0.05 * jax.random.normal(jax.random.fold_in(_tk, 500 + 24), (1000, 128), jnp.float32)
        tbl_25 = 0.05 * jax.random.normal(jax.random.fold_in(_tk, 500 + 25), (1250, 128), jnp.float32)
        _rk = jax.random.fold_in(_tk, 7)
        r_dense_features = -0.000520686 + 1.00062 * jax.random.normal(jax.random.fold_in(_rk, 101), (2048, 128), jnp.float32)
        W_top1 = 0.0405887 * jax.random.normal(jax.random.fold_in(_tk, 801), (607, 512), jnp.float32)
        W_top2 = 0.0441942 * jax.random.normal(jax.random.fold_in(_tk, 802), (512, 256), jnp.float32)
        W_top3 = 0.0625 * jax.random.normal(jax.random.fold_in(_tk, 803), (256, 1), jnp.float32)
        b_top1 = jnp.zeros((512,), jnp.float32)
        b_top2 = jnp.zeros((256,), jnp.float32)
        return (r_dense_features, ids, tbl_0, tbl_1, tbl_2, tbl_3, tbl_4, tbl_5, tbl_6, tbl_7, tbl_8, tbl_9, tbl_10, tbl_11, tbl_12, tbl_13, tbl_14, tbl_15, tbl_16, tbl_17, tbl_18, tbl_19, tbl_20, tbl_21, tbl_22, tbl_23, tbl_24, tbl_25, W_top1, b_top1, W_top2, b_top2, W_top3)
    r_dense_features, ids, tbl_0, tbl_1, tbl_2, tbl_3, tbl_4, tbl_5, tbl_6, tbl_7, tbl_8, tbl_9, tbl_10, tbl_11, tbl_12, tbl_13, tbl_14, tbl_15, tbl_16, tbl_17, tbl_18, tbl_19, tbl_20, tbl_21, tbl_22, tbl_23, tbl_24, tbl_25, W_top1, b_top1, W_top2, b_top2, W_top3 = _rec_inputs()

    def _L0_rec_setup():
        import jax, jax.numpy as jnp
        import numpy as np
        F = 26
        key = jax.random.key(seed)
        k1, k2 = jax.random.split(key)
        B, D = (2048, 128)
        dense_features = jax.random.normal(k1, (B, D), dtype=jnp.float32)
        sparse_features = jax.random.normal(k2, (B, F, D), dtype=jnp.float32)
        return {'dense_features': dense_features, 'sparse_features': sparse_features}
    _L0_rec_all = _L0_rec_setup()
    _L0_rec_in = {k: v for k, v in _L0_rec_all.items() if k in ()}
    del _L0_rec_all
    return {'r_dense_features': r_dense_features, 'ids': ids, 'tbl_0': tbl_0, 'tbl_1': tbl_1, 'tbl_2': tbl_2, 'tbl_3': tbl_3, 'tbl_4': tbl_4, 'tbl_5': tbl_5, 'tbl_6': tbl_6, 'tbl_7': tbl_7, 'tbl_8': tbl_8, 'tbl_9': tbl_9, 'tbl_10': tbl_10, 'tbl_11': tbl_11, 'tbl_12': tbl_12, 'tbl_13': tbl_13, 'tbl_14': tbl_14, 'tbl_15': tbl_15, 'tbl_16': tbl_16, 'tbl_17': tbl_17, 'tbl_18': tbl_18, 'tbl_19': tbl_19, 'tbl_20': tbl_20, 'tbl_21': tbl_21, 'tbl_22': tbl_22, 'tbl_23': tbl_23, 'tbl_24': tbl_24, 'tbl_25': tbl_25, 'W_top1': W_top1, 'b_top1': b_top1, 'W_top2': W_top2, 'b_top2': b_top2, 'W_top3': W_top3}

def reference(r_dense_features, ids, tbl_0, tbl_1, tbl_2, tbl_3, tbl_4, tbl_5, tbl_6, tbl_7, tbl_8, tbl_9, tbl_10, tbl_11, tbl_12, tbl_13, tbl_14, tbl_15, tbl_16, tbl_17, tbl_18, tbl_19, tbl_20, tbl_21, tbl_22, tbl_23, tbl_24, tbl_25, W_top1, b_top1, W_top2, b_top2, W_top3):
    import jax
    import jax.numpy as jnp

    def _L0_rec_ref(dense_features, sparse_features):
        import jax, jax.numpy as jnp
        import numpy as np
        F = 26
        B, D = dense_features.shape
        combined = jnp.concatenate((dense_features[:, None, :], sparse_features), axis=1)
        interactions = jnp.einsum('bfd,bgd->bfg', combined, combined)
        iu, ju = jnp.triu_indices(F + 1, k=1)
        interactions_flat = interactions[:, iu, ju]
        return jnp.concatenate((dense_features, interactions_flat), axis=1)
    e = jnp.stack([tbl_0[ids[:, 0]], tbl_1[ids[:, 1]], tbl_2[ids[:, 2]], tbl_3[ids[:, 3]], tbl_4[ids[:, 4]], tbl_5[ids[:, 5]], tbl_6[ids[:, 6]], tbl_7[ids[:, 7]], tbl_8[ids[:, 8]], tbl_9[ids[:, 9]], tbl_10[ids[:, 10]], tbl_11[ids[:, 11]], tbl_12[ids[:, 12]], tbl_13[ids[:, 13]], tbl_14[ids[:, 14]], tbl_15[ids[:, 15]], tbl_16[ids[:, 16]], tbl_17[ids[:, 17]], tbl_18[ids[:, 18]], tbl_19[ids[:, 19]], tbl_20[ids[:, 20]], tbl_21[ids[:, 21]], tbl_22[ids[:, 22]], tbl_23[ids[:, 23]], tbl_24[ids[:, 24]], tbl_25[ids[:, 25]]], axis=1)
    z = _L0_rec_ref(r_dense_features, e)
    z = z.reshape(z.shape[0], -1)
    h = jnp.concatenate([z, r_dense_features], axis=1)
    h = jnp.maximum(h @ W_top1 + b_top1, 0.0)
    h = jnp.maximum(h @ W_top2 + b_top2, 0.0)
    y = h @ W_top3
    return y

_drawn_inputs = setup_inputs


def setup_inputs(seed=0):
    import zlib

    import numpy as np

    out = dict(_drawn_inputs(seed))
    spreads = {'b_top1': (0.0, 0.1), 'b_top2': (0.0, 0.1)}
    factors = {}
    for name, (base, spread) in spreads.items():
        noise = np.random.default_rng([zlib.crc32(name.encode()), seed]).standard_normal(out[name].shape)
        drawn = base * np.exp(spread * noise) if base else spread * noise
        out[name] = jnp.asarray(drawn.astype(out[name].dtype))
    for name, factor in factors.items():
        out[name] = (out[name] * factor).astype(out[name].dtype)
    return out
```

```python
import numpy as np
import concourse.bass as bass
from concourse import mybir
from contextlib import ExitStack

F32 = mybir.dt.float32
F32R = mybir.dt.float32r
I32 = mybir.dt.int32
ALU = mybir.AluOpType
ACT = mybir.ActivationFunctionType

P = 128
D = 128
BATCH = 2048
TILES = BATCH // P
JT = 4
BLOCKS = TILES // JT
BS = JT * P

N_TABLES = 26
SMALL = (10, 13, 17, 19, 21, 23, 24)
LARGE = tuple(f for f in range(N_TABLES) if f not in SMALL)
SMALL_ROWS = 1000
CH = 8
CP = SMALL_ROWS // CH
NS, NG = len(SMALL), len(LARGE)
FIXED = 1 + NS
SLOTS = FIXED + NG
ORDER = (0,) + tuple(1 + f for f in SMALL) + tuple(1 + f for f in LARGE)

W = 32
GS = 4
GROUPS = P // GS
BANK = 512
GB = 4
BUF_BANKS = 2
BUF_GROUPS = GB * BUF_BANKS
BUFS = GROUPS // BUF_GROUPS

PAIRS = SLOTS * (SLOTS - 1) // 2
DELTAS = PAIRS // SLOTS
XW = SLOTS + DELTAS
PC = 3
PR = PAIRS // PC
H1, H2 = 512, 256
N1, N2 = H1 // P, H2 // P

TB = 4
TURNS = [(i, min(TB, NG - i)) for i in range(0, NG, TB)]
NT = len(TURNS)
STEP_TABLES = [(None, 0), (1, 2), (3, 4), (5, 6)]


def uses(j, look_up=True):
    return sum(NT + look_up * sum(k is not None for k in STEP_TABLES[i]) for i in range(j))


START_USES = NS + NT
BLOCK_USES = uses(JT)


def tower_program(nc, gather_ids, small_ids, dense_cols, dense_rows, small_tables, large_tables,
                  w_pairs, w_dense, w_dense2, w2, w3, b1, b2, y):
    ctx = ExitStack()
    with ctx:
        def sb(name, shape, dt=F32):
            return ctx.enter_context(nc.sbuf_tensor(name, shape, dt))

        def sem(name):
            return ctx.enter_context(nc.semaphore(name))

        rows = [sb(f"rows{i}", [P, NG, D]) for i in range(2)]
        feats = [sb(f"feats{i}", [P, P * W]) for i in range(2)]
        fixed = sb("fixed", [P, FIXED, 2 * BS])
        onehot = [sb(f"onehot{i}", [CP, CH, BS], F32R) for i in range(2)]
        table_hi = sb("table_hi", [CP, NS, CH * D], F32R)
        table_lo = sb("table_lo", [CP, NS, CH * D], F32R)
        wanted = [sb(f"wanted{i}", [CP, BS], I32) for i in range(2)]
        row_no_i = sb("row_no_i", [CP, CH], I32)
        row_no = sb("row_no", [CP, CH])
        ids = [sb(f"ids{i}", [P, NG], I32) for i in range(JT)]
        ident = sb("ident", [P, P])
        diag = sb("diag", [P, SLOTS * GROUPS])
        table = sb("table", [P, W * XW])
        pairs = sb("pairs", [P, PAIRS])
        pairs_t = sb("pairs_t", [PR, PC * P])
        dense = [sb(f"dense{i}", [P, P]) for i in range(JT)]
        w1_sb = sb("w1_sb", [P, (PC + 1) * H1])
        w2_sb = sb("w2_sb", [P, N1 * H2])
        w3_sb = sb("w3_sb", [P, N2])
        b1_sb = sb("b1_sb", [P, N1])
        b2_sb = sb("b2_sb", [P, N2])
        h1 = sb("h1", [P, N1 * P])
        h2 = sb("h2", [P, N2 * P])
        y_sb = sb("y_sb", [1, P])

        turn = [ctx.enter_context(nc.psum_tensor(f"turn{i}", [P, BANK], F32)) for i in range(2)]
        prod = [ctx.enter_context(nc.psum_tensor(f"prod{i}", [P, BUF_BANKS * BANK], F32)) for i in range(2)]
        mlp_a = ctx.enter_context(nc.psum_tensor("mlp_a", [P, BANK], F32))
        mlp_b = ctx.enter_context(nc.psum_tensor("mlp_b", [P, BANK], F32))

        ids_in = [sem(f"ids_in{i}") for i in range(JT)]
        gather_begun = sem("gather_begun")
        gathered = [sem(f"gathered{i}") for i in range(2)]
        wanted_in = [sem(f"wanted_in{i}") for i in range(2)]
        raw_in = [sem(f"raw_in{k}") for k in range(NS)]
        dense_cols_in = sem("dense_cols_in")
        dense_in = [sem(f"dense_in{i}") for i in range(JT)]
        w_dense_in = sem("w_dense_in")
        w_in = sem("w_in")
        w1_ready = sem("w1_ready")
        ident_zero = sem("ident_zero")
        ident_ready = sem("ident_ready")
        row_no_made = sem("row_no_made")
        row_no_ready = sem("row_no_ready")
        pads_ready = sem("pads_ready")
        hi_ready = sem("hi_ready")
        lo_ready = sem("lo_ready")
        onehot_ready = sem("onehot_ready")
        turn_full = sem("turn_full")
        turn_read = sem("turn_read")
        fixed_placed = sem("fixed_placed")
        prod_full = sem("prod_full")
        prod_read_v = sem("prod_read_v")
        prod_read_s = sem("prod_read_s")
        table_made = sem("table_made")
        table_wrapped = sem("table_wrapped")
        pairs_ready = sem("pairs_ready")
        pairs_turned = sem("pairs_turned")
        pairs_t_ready = sem("pairs_t_ready")
        l1_full = sem("l1_full")
        h1_ready = sem("h1_ready")
        l2_full = sem("l2_full")
        h2_ready = sem("h2_ready")
        l3_full = sem("l3_full")
        y_ready = sem("y_ready")
        y_stored = sem("y_stored")

        def feats_by_slot(i):
            return feats[i][:, :].rearrange("d (b w) -> d w b", w=W)

        block = ctx.enter_context(nc.Block())

        @block.sync
        def _(sp):
            def load_wanted(blk, k):
                v = NS * blk + k
                if not (isinstance(v, int) and v < 2):
                    sp.wait_ge(onehot_ready, v if k == 0 else v - 1)
                sp.dma_start(wanted[k % 2][:, :], small_ids[bass.ds(blk, 1), k, :].broadcast_to([CP, BS]))\
                    .then_inc(wanted_in[k % 2], 16)

            for j in range(JT):
                sp.dma_start(ids[j][:, :], gather_ids[j]).then_inc(ids_in[j], 16)
            for k in range(NS):
                if k < 2:
                    load_wanted(0, k)
                sp.dma_start(fixed[0:CP, 1 + k, :], small_tables[k].rearrange("(p c) d -> p (c d)", c=CH))\
                    .then_inc(raw_in[k], 16)
            sp.dma_start(fixed[:, 0, 0:BS], dense_cols[0]).then_inc(dense_cols_in, 16)
            sp.dma_start(w1_sb[0:PR, 0:PC * H1].rearrange("p (c n) -> p c n", c=PC),
                         w_pairs.rearrange("c p n -> p c n")).then_inc(w_in, 16)
            sp.dma_start(w1_sb[:, PC * H1:], w_dense).then_inc(w_dense_in, 16)
            sp.dma_start(table[:, 0:H1], w_dense2).then_inc(w_dense_in, 16)
            sp.dma_start(w2_sb[:, :].rearrange("p (c n) -> p c n", c=N1),
                         w2.rearrange("(c p) n -> p c n", c=N1)).then_inc(w_in, 16)
            sp.dma_start(w3_sb[:, :], w3).then_inc(w_in, 16)
            sp.dma_start(b1_sb[:, :], b1).then_inc(w_in, 16)
            sp.dma_start(b2_sb[:, :], b2).then_inc(w_in, 16)
            for k in range(2, NS):
                load_wanted(0, k)
                if k < 2 + JT:
                    sp.dma_start(dense[k - 2][:, :], dense_rows[k - 2]).then_inc(dense_in[k - 2], 16)

            with sp.Fori(0, BLOCKS - 1) as b:
                load_wanted(b + 1, 0)
                load_wanted(b + 1, 1)
                sp.wait_ge(fixed_placed, JT * b)
                sp.wait_ge(dense_cols_in, 16 * b + 16)
                sp.dma_start(fixed[:, 0, bass.ds(BS * ((b + 1) % 2), BS)], dense_cols[bass.ds(b + 1, 1)]
                             .rearrange("a p n -> (a p) n")).then_inc(dense_cols_in, 16)
                for j in range(JT):
                    for k in {0: (2, 3), 1: (4, 5), 2: (6,), 3: ()}[j]:
                        load_wanted(b + 1, k)
                    sp.wait_ge(gathered[j % 2], 16 * NG * (2 * b + j // 2 + 1))
                    sp.dma_start(ids[j][:, :], gather_ids[bass.ds(JT * b + JT + j, 1)]
                                 .rearrange("a p n -> (a p) n")).then_inc(ids_in[j], 16)
                    sp.wait_ge(l1_full, JT * b + j + 1)
                    sp.dma_start(dense[j][:, :], dense_rows[bass.ds(JT * b + JT + j, 1)]
                                 .rearrange("a p n -> (a p) n")).then_inc(dense_in[j], 16)

        @block.gpsimd
        def _(gp):
            gp.iota(row_no_i[:, :], pattern=[[1, CH]], base=0, channel_multiplier=CH).then_inc(row_no_made, 1)
            gp.memset(ident[:, :], 0.0).then_inc(ident_zero, 1)

            def gather(j, ids_use):
                gp.wait_ge(ids_in[j], 16 * ids_use)
                gp.sem_inc(gather_begun, 1)
                for g in range(NG):
                    gp.indirect_dma_start(rows[j % 2][:, g, :], None, large_tables[g],
                                          bass.IndirectOffsetOnAxis(ap=ids[j][:, g:g + 1], axis=0))\
                        .then_inc(gathered[j % 2], 16)

            gather(0, 1)
            gp.wait_ge(ident_zero, 1)
            gp.affine_select(out=ident[:, :], in_=ident[:, :], compare_op=ALU.not_equal, fill=1.0,
                             base=0, pattern=[[-1, P]], channel_multiplier=1).then_inc(ident_ready, 1)
            gather(1, 1)

            def refill(b, i):
                gp.wait_ge(turn_full, START_USES + BLOCK_USES * b + (uses(i - 1) + NT if i else 0))
                gather((2 + i) % JT, b + 1 + (2 + i) // JT)

            with gp.Fori(0, BLOCKS - 1) as b:
                for i in range(JT):
                    refill(b, i)
            for i in range(2):
                refill(BLOCKS - 1, i)

        @block.scalar
        def _(act):
            def empty_bank(local, full, out, src):
                act.wait_ge(turn_full, full)
                nc.scalar.activation(out, src(turn[local % 2]), ACT.Copy).then_inc(turn_read, 1)

            def empty_features(i, local, base):
                for n, (g, m) in enumerate(TURNS):
                    empty_bank(local + n, base + local + n + 1, feats_by_slot(i)[:, FIXED + g:FIXED + g + m, :],
                               lambda bank: bank[:, 0:m * P].rearrange("d (f b) -> d f b", f=m))

            def empty_lookup(k, half, local, base):
                empty_bank(local, base + local + 1, fixed[:, 1 + k, bass.ds(BS * half, BS)], lambda bank: bank[:, :])

            def read_products(tile, i):
                act.wait_ge(prod_full, BUFS * tile + i + 1)
                for s in (2, 3):
                    last = nc.scalar.activation(diag_part(diag, s, i), prod_part(prod[i % 2], s), ACT.Copy)
                last.then_inc(prod_read_s, 1)

            for k in range(NS):
                act.wait_ge(raw_in[k], 16)
                nc.scalar.activation(table_hi[:, k, :], fixed[0:CP, 1 + k, :], ACT.Copy).then_inc(hi_ready, 1)
                if k:
                    empty_lookup(k - 1, 0, k - 1, 0)
            empty_lookup(NS - 1, 0, NS - 1, 0)
            act.wait_ge(pads_ready, 2)
            empty_features(0, NS, 0)
            for i in range(BUFS):
                read_products(0, i)
            act.wait_ge(w_in, 5 * 16)

            def step(b, j, look_up, front):
                base = START_USES + BLOCK_USES * b
                t = JT * b + j
                local = uses(j, look_up)
                if front:
                    empty_features((j + 1) % 2, local, base)
                    local += NT
                if look_up and STEP_TABLES[j][0] is not None:
                    empty_lookup(STEP_TABLES[j][0], (b + 1) % 2, local, base)
                    local += 1
                act.wait_ge(pairs_turned, t + 1)
                nc.scalar.activation(pairs_t[:, :], mlp_a[0:PR, 0:PC * P], ACT.Copy).then_inc(pairs_t_ready, 1)
                if look_up:
                    empty_lookup(STEP_TABLES[j][1], (b + 1) % 2, local, base)
                act.wait_ge(l1_full, t + 1)
                for n in range(N1):
                    last = nc.scalar.activation(h1[:, n * P:(n + 1) * P], mlp_b[:, n * P:(n + 1) * P], ACT.Relu,
                                                bias=b1_sb[:, n:n + 1])
                last.then_inc(h1_ready, 1)
                if front:
                    read_products(t + 1, 0)
                    read_products(t + 1, 1)
                act.wait_ge(l2_full, t + 1)
                for n in range(N2):
                    last = nc.scalar.activation(h2[:, n * P:(n + 1) * P], mlp_a[:, n * P:(n + 1) * P], ACT.Relu,
                                                bias=b2_sb[:, n:n + 1])
                last.then_inc(h2_ready, 1)
                if front:
                    read_products(t + 1, 2)
                    read_products(t + 1, 3)
                act.wait_ge(l3_full, t + 1)
                act.wait_ge(y_stored, 16 * t)
                nc.scalar.activation(y_sb[:, :], mlp_a[0:1, N2 * P:(N2 + 1) * P], ACT.Copy).then_inc(y_ready, 1)
                act.wait_ge(y_ready, t + 1)
                act.dma_start(y[bass.ds(t, 1), :], y_sb[:, :]).then_inc(y_stored, 16)

            with act.Fori(0, BLOCKS - 1) as b:
                for j in range(JT):
                    step(b, j, True, True)
            for j in range(JT):
                step(BLOCKS - 1, j, False, j < JT - 1)
            act.wait_ge(y_stored, 16 * TILES)

        @block.vector
        def _(dve):
            def one_hot(k, cs, use):
                if cs[0] == 0:
                    dve.wait_ge(wanted_in[k % 2], 16 * use)
                for c in cs:
                    made = nc.vector.tensor_scalar(onehot[k % 2][:, c, :], wanted[k % 2][:, :], row_no[:, c:c + 1],
                                                   None, ALU.is_equal)
                if cs[-1] == CH - 1:
                    made.then_inc(onehot_ready, 1)

            def place_fixed(i, j, half):
                nc.vector.tensor_copy(feats_by_slot(i)[:, 0:FIXED, :],
                                      fixed[:, :, bass.ds(BS * half + j * P, P)]).then_inc(fixed_placed, 1)

            def read_products(tile, i):
                dve.wait_ge(prod_full, BUFS * tile + i + 1)
                for s in (0, 1):
                    last = nc.vector.tensor_copy(diag_part(diag, s, i), prod_part(prod[i % 2], s))
                last.then_inc(prod_read_v, 1)

            def make_pairs(tile):
                dve.wait_ge(prod_read_v, BUFS * (tile + 1))
                dve.wait_ge(prod_read_s, BUFS * (tile + 1))
                nc.vector.transpose(table[:, :].rearrange("p (f g) -> p g f", g=XW)[:, 0:SLOTS, :],
                                    diag[:, :].rearrange("p (g n) -> p g n", n=GROUPS)).then_inc(table_made, 1)
                dve.wait_ge(table_made, tile + 1)
                rows_of = table[:, :].rearrange("p (f g) -> p f g", g=XW)[:, SLOTS - DELTAS:SLOTS, :]
                nc.vector.tensor_copy(rows_of[:, :, SLOTS:XW], rows_of[:, :, 0:DELTAS]).then_inc(table_wrapped, 1)
                dve.wait_ge(table_wrapped, tile + 1)
                if not (isinstance(tile, int) and tile == 0):
                    dve.wait_ge(pairs_turned, tile)
                nc.vector.tensor_copy(pairs[:, :].rearrange("p (f k) -> p f k", k=DELTAS),
                                      table[:, 1:1 + SLOTS * (XW + 1)]
                                      .rearrange("p (f g) -> p f g", g=XW + 1)[:, :, 0:DELTAS])\
                    .then_inc(pairs_ready, 1)

            dve.wait_ge(row_no_made, 1)
            nc.vector.tensor_copy(row_no[:, :], row_no_i[:, :]).then_inc(row_no_ready, 1)
            dve.wait_ge(row_no_ready, 1)
            for k in range(NS):
                if k >= 2:
                    dve.wait_ge(turn_full, k - 1)
                one_hot(k, range(CH), k // 2 + 1)
                dve.wait_ge(hi_ready, k + 1)
                nc.vector.tensor_tensor(table_lo[:, k, :], fixed[0:CP, 1 + k, :],
                                        table_hi[:, k, :].bitcast(F32), ALU.subtract).then_inc(lo_ready, 1)
                if k == 0:
                    for i in range(2):
                        nc.vector.memset(feats[i][:, :].rearrange("d (b w) -> d b w", w=W)[:, :, SLOTS:W], 0.0)\
                            .then_inc(pads_ready, 1)
            dve.wait_ge(w_dense_in, 32)
            nc.vector.tensor_tensor(w1_sb[:, PC * H1:], w1_sb[:, PC * H1:], table[:, 0:H1], ALU.add)\
                .then_inc(w1_ready, 1)
            dve.wait_ge(turn_read, NS)
            dve.wait_ge(dense_cols_in, 16)
            place_fixed(0, 0, 0)
            for i in range(BUFS):
                read_products(0, i)
            make_pairs(0)

            def step(b, j, look_up, front):
                base = START_USES + BLOCK_USES * b
                t = JT * b + j
                before = [4 * (b + 1), 3 * (b + 1)]
                if front:
                    if j == JT - 1:
                        dve.wait_ge(turn_read, base + BLOCK_USES)
                        dve.wait_ge(dense_cols_in, 16 * (b + 2))
                    dve.wait_ge(prod_full, BUFS * t)
                    place_fixed((j + 1) % 2, (j + 1) % JT, b % 2 if j < JT - 1 else (b + 1) % 2)
                if look_up and j == 0:
                    dve.wait_ge(turn_full, base)
                    one_hot(0, range(CH), before[0] + 1)
                nxt = STEP_TABLES[j + 1] if look_up and j < JT - 1 else None
                if nxt:
                    if j:
                        dve.wait_ge(turn_full, base + uses(j) + NT + 1)
                    one_hot(nxt[0], range(CH), before[1] + nxt[0] // 2 + 1)
                for i in range(BUFS):
                    if front:
                        read_products(t + 1, i)
                    if nxt:
                        if i == 0:
                            dve.wait_ge(turn_full, base + uses(j + 1))
                        one_hot(nxt[1], range(2 * i, 2 * i + 2), before[0] + nxt[1] // 2 + 1)
                if front:
                    make_pairs(t + 1)

            with dve.Fori(0, BLOCKS - 1) as b:
                for j in range(JT):
                    step(b, j, True, True)
            for j in range(JT - 1):
                step(BLOCKS - 1, j, False, True)

        @block.tensor
        def _(pe):
            def turn_bank(local, total, first):
                need = total if first else total - 1
                if not (isinstance(need, int) and need < 1):
                    pe.wait_ge(turn_read, need)
                return turn[local % 2]

            def turn_features(i, arrivals, local, base, first):
                pe.wait_ge(gathered[i], 16 * NG * arrivals)
                for n, (g, m) in enumerate(TURNS):
                    bank = turn_bank(local + n, base + local + n, first and n == 0)
                    for f in range(m):
                        last = nc.tensor.transpose(bank[:, f * P:(f + 1) * P], rows[i][:, g + f, :], ident[:, :])
                    last.then_inc(turn_full, 1)

            def look_up_table(k, ready, local, base):
                bank = turn_bank(local, base + local, False)
                pe.wait_ge(onehot_ready, ready)
                for c in range(CH):
                    for part in (table_hi, table_lo):
                        last = nc.tensor.matmul(bank[:, :], part[:, k, c * D:(c + 1) * D], onehot[k % 2][:, c, :],
                                                start=(c == 0 and part is table_hi),
                                                stop=(c == CH - 1 and part is table_lo))
                last.then_inc(turn_full, 1)

            def products(tile, parity, i):
                n = BUFS * tile + i
                if not (isinstance(n, int) and n < 2):
                    pe.wait_ge(prod_read_v, n - 1)
                    pe.wait_ge(prod_read_s, n - 1)
                x = feats[parity]
                for g in range(BUF_GROUPS):
                    own = x[:, (i * BUF_GROUPS + g) * P:(i * BUF_GROUPS + g + 1) * P]
                    at = (g // GB) * BANK + (g % GB) * GS * SLOTS
                    last = nc.tensor.matmul(prod[i % 2][:, at:at + GS * SLOTS], own,
                                            own.rearrange("d (s w) -> d s w", w=W)[:, :, 0:SLOTS],
                                            start=True, stop=True)
                last.then_inc(prod_full, 1)

            for k in range(NS):
                pe.wait_ge(lo_ready, k + 1)
                look_up_table(k, k + 1, k, 0)
            pe.wait_ge(ident_ready, 1)
            turn_features(0, 1, NS, 0, False)
            pe.wait_ge(turn_read, START_USES)
            pe.wait_ge(fixed_placed, 1)
            for i in range(BUFS):
                products(0, 0, i)
            pe.wait_ge(w1_ready, 1)
            pe.wait_ge(w_in, 5 * 16)

            def step(b, j, look_up, front):
                base = START_USES + BLOCK_USES * b
                t = JT * b + j
                local = uses(j, look_up)
                if front:
                    turn_features((j + 1) % 2, 2 * b + (j + 1) // 2 + 1, local, base, j == 0)
                    local += NT
                turned = base + local
                if look_up and STEP_TABLES[j][0] is not None:
                    k = STEP_TABLES[j][0]
                    look_up_table(k, NS * (b + 1) + k + 1, local, base)
                    local += 1
                pe.wait_ge(pairs_ready, t + 1)
                pe.wait_ge(y_ready, t)
                for c in range(PC):
                    last = nc.tensor.transpose(mlp_a[0:PR, c * P:(c + 1) * P], pairs[:, c * PR:(c + 1) * PR],
                                               ident[:, :])
                last.then_inc(pairs_turned, 1)
                if look_up:
                    k = STEP_TABLES[j][1]
                    look_up_table(k, NS * (b + 1) + k + 1, local, base)
                pe.wait_ge(pairs_t_ready, t + 1)
                pe.wait_ge(dense_in[j], 16 * (b + 1))
                for n in range(N1):
                    for c in range(PC):
                        nc.tensor.matmul(mlp_b[:, n * P:(n + 1) * P], w1_sb[0:PR, c * H1 + n * P:c * H1 + (n + 1) * P],
                                         pairs_t[:, c * P:(c + 1) * P], start=(c == 0), stop=False)
                    last = nc.tensor.matmul(mlp_b[:, n * P:(n + 1) * P],
                                            w1_sb[:, PC * H1 + n * P:PC * H1 + (n + 1) * P],
                                            dense[j][:, :], start=False, stop=True)
                last.then_inc(l1_full, 1)
                if front:
                    pe.wait_ge(turn_read, turned)
                    pe.wait_ge(fixed_placed, t + 2)
                    products(t + 1, (j + 1) % 2, 0)
                    products(t + 1, (j + 1) % 2, 1)
                pe.wait_ge(h1_ready, t + 1)
                for n in range(N2):
                    for c in range(N1):
                        last = nc.tensor.matmul(mlp_a[:, n * P:(n + 1) * P],
                                                w2_sb[:, c * H2 + n * P:c * H2 + (n + 1) * P],
                                                h1[:, c * P:(c + 1) * P], start=(c == 0), stop=(c == N1 - 1))
                last.then_inc(l2_full, 1)
                if front:
                    products(t + 1, (j + 1) % 2, 2)
                    products(t + 1, (j + 1) % 2, 3)
                pe.wait_ge(h2_ready, t + 1)
                for c in range(N2):
                    last = nc.tensor.matmul(mlp_a[0:1, N2 * P:(N2 + 1) * P], w3_sb[:, c:c + 1],
                                            h2[:, c * P:(c + 1) * P], start=(c == 0), stop=(c == N2 - 1))
                last.then_inc(l3_full, 1)

            with pe.Fori(0, BLOCKS - 1) as b:
                for j in range(JT):
                    step(b, j, True, True)
            for j in range(JT):
                step(BLOCKS - 1, j, False, j < JT - 1)


def prod_part(buf, s):
    return buf[W * s:W * (s + 1), :].rearrange("p (k r) -> p k r", k=BUF_BANKS)[:, :, 0:GB * GS * SLOTS]\
        .rearrange("p k (g r) -> p k g r", g=GB)[:, :, :, s * SLOTS:(s + 1) * SLOTS]


def diag_part(diag, s, i):
    return diag[W * s:W * (s + 1), :].rearrange("p (f n) -> p n f", n=GROUPS)[
        :, i * BUF_GROUPS:(i + 1) * BUF_GROUPS, :].rearrange("p (k g) f -> p k g f", k=BUF_BANKS)


def kernel(**inputs):
    import concourse.bacc as bacc
    from concourse import mybir as _mybir
    from concourse.bass_utils import run_bass_kernel_spmd

    arr = {k: np.ascontiguousarray(v) for k, v in inputs.items()}
    ids, x, w1 = arr["ids"], arr["r_dense_features"], arr["W_top1"]

    by_column = ids.reshape(TILES, GS, GROUPS, N_TABLES).transpose(0, 2, 1, 3).reshape(TILES, P, N_TABLES)
    x_column = x.reshape(TILES, GS, GROUPS, D).transpose(0, 2, 1, 3).reshape(BLOCKS, BS, D)
    first = np.arange(SLOTS).repeat(DELTAS)
    second = (first + np.tile(np.arange(1, DELTAS + 1), SLOTS)) % SLOTS
    a, c = np.array(ORDER)[first], np.array(ORDER)[second]
    lo, hi = np.minimum(a, c), np.maximum(a, c)
    pair_row = D + lo * SLOTS - lo * (lo + 1) // 2 + hi - lo - 1

    feeds = {
        "gather_ids": by_column[:, :, list(LARGE)],
        "small_ids": by_column.reshape(BLOCKS, BS, N_TABLES)[:, :, list(SMALL)].transpose(0, 2, 1),
        "dense_cols": x_column.transpose(0, 2, 1),
        "dense_rows": x.reshape(TILES, P, D).transpose(0, 2, 1),
        **{f"tbl_{f}": arr[f"tbl_{f}"] for f in range(N_TABLES)},
        "w_pairs": w1[pair_row].reshape(PC, PR, H1),
        "w_dense": w1[:D],
        "w_dense2": w1[D + PAIRS:],
        "w2": arr["W_top2"],
        "w3": arr["W_top3"].reshape(N2, P).T,
        "b1": arr["b_top1"].reshape(N1, P).T,
        "b2": arr["b_top2"].reshape(N2, P).T,
    }
    feeds = {f"in_{k}": np.ascontiguousarray(v) for k, v in feeds.items()}
    nc = bacc.Bacc("TRN2", target_bir_lowering=False, num_devices=1)
    ap = {k: nc.dram_tensor(k, v.shape, _mybir.dt.from_np(v.dtype), kind="ExternalInput").ap()
          for k, v in feeds.items()}
    y = nc.dram_tensor("out_y", (TILES, P), F32, kind="ExternalOutput").ap()
    tower_program(nc, ap["in_gather_ids"], ap["in_small_ids"], ap["in_dense_cols"], ap["in_dense_rows"],
                  [ap[f"in_tbl_{f}"] for f in SMALL], [ap[f"in_tbl_{f}"] for f in LARGE],
                  ap["in_w_pairs"], ap["in_w_dense"], ap["in_w_dense2"], ap["in_w2"], ap["in_w3"],
                  ap["in_b1"], ap["in_b2"], y)
    r = run_bass_kernel_spmd(nc, [feeds], core_ids=[0])
    return r.results[0]["out_y"].reshape(BATCH, 1)
```

```python
import numpy as np
import concourse.bass as bass
from concourse import mybir
from contextlib import ExitStack

F32 = mybir.dt.float32
F32R = mybir.dt.float32r
I32 = mybir.dt.int32
ALU = mybir.AluOpType
ACT = mybir.ActivationFunctionType

P = 128
D = 128
BATCH = 2048
TILES = BATCH // P
JT = 4
BLOCKS = TILES // JT
BS = JT * P

N_TABLES = 26
SMALL = (10, 13, 17, 19, 21, 23, 24)
LARGE = tuple(f for f in range(N_TABLES) if f not in SMALL)
SMALL_ROWS = 1000
CH = 8
CP = SMALL_ROWS // CH
NS, NG = len(SMALL), len(LARGE)
FIXED = 1 + NS
SLOTS = FIXED + NG
ORDER = (0,) + tuple(1 + f for f in SMALL) + tuple(1 + f for f in LARGE)

W = 32
GS = 4
GROUPS = P // GS
BANK = 512
GB = 4
BUF_BANKS = 2
BUF_GROUPS = GB * BUF_BANKS
BUFS = GROUPS // BUF_GROUPS

PAIRS = SLOTS * (SLOTS - 1) // 2
DELTAS = PAIRS // SLOTS
XW = SLOTS + DELTAS
PC = 3
PR = PAIRS // PC
H1, H2 = 512, 256
N1, N2 = H1 // P, H2 // P

TB = 4
TURNS = [(i, min(TB, NG - i)) for i in range(0, NG, TB)]
NT = len(TURNS)

EVEN = (NS + 1) // 2
ODD = NS // 2


def uses(j, look_up=True):
    return j * (NT + look_up)


START_USES = EVEN + NT
BLOCK_USES = uses(JT)


def tower_program(nc, gather_ids, small_ids, dense_cols, dense_rows, small_tables, large_tables,
                  w_pairs, w_dense, w_dense2, w2, w3, b1, b2, y):
    ctx = ExitStack()
    with ctx:
        def sb(name, shape, dt=F32):
            return ctx.enter_context(nc.sbuf_tensor(name, shape, dt))

        def sem(name):
            return ctx.enter_context(nc.semaphore(name))

        rows = [sb(f"rows{i}", [P, NG, D]) for i in range(2)]
        feats = [sb(f"feats{i}", [P, P * W]) for i in range(2)]
        fixed = sb("fixed", [P, FIXED, 2 * BS])
        onehot = [sb(f"onehot{i}", [CP, CH, BS], F32R) for i in range(2)]
        table_hi = sb("table_hi", [CP, NS, CH * D], F32R)
        table_lo = sb("table_lo", [CP, NS, CH * D], F32R)
        wanted = [sb(f"wanted{i}", [CP, BS], I32) for i in range(2)]
        row_no_i = sb("row_no_i", [CP, CH], I32)
        row_no = sb("row_no", [CP, CH])
        ids = [sb(f"ids{i}", [P, NG], I32) for i in range(JT)]
        ident = sb("ident", [P, P])
        diag = sb("diag", [P, SLOTS * GROUPS])
        table = sb("table", [P, W * XW])
        pairs = sb("pairs", [P, PAIRS])
        pairs_t = sb("pairs_t", [PR, PC * P])
        dense = [sb(f"dense{i}", [P, P]) for i in range(JT)]
        w1_sb = sb("w1_sb", [P, (PC + 1) * H1])
        w2_sb = sb("w2_sb", [P, N1 * H2])
        w3_sb = sb("w3_sb", [P, N2])
        b1_sb = sb("b1_sb", [P, N1])
        b2_sb = sb("b2_sb", [P, N2])
        h1 = sb("h1", [P, N1 * P])
        h2 = sb("h2", [P, N2 * P])
        y_sb = sb("y_sb", [1, 2 * P])

        turn = [ctx.enter_context(nc.psum_tensor(f"turn{i}", [P, BANK], F32)) for i in range(2)]
        prod = [ctx.enter_context(nc.psum_tensor(f"prod{i}", [P, BUF_BANKS * BANK], F32)) for i in range(2)]
        mlp_a = ctx.enter_context(nc.psum_tensor("mlp_a", [P, BANK], F32))
        mlp_b = ctx.enter_context(nc.psum_tensor("mlp_b", [P, BANK], F32))

        ids_in = [sem(f"ids_in{i}") for i in range(JT)]
        gather_begun = sem("gather_begun")
        gathered = [sem(f"gathered{i}") for i in range(2)]
        wanted_in = [sem(f"wanted_in{i}") for i in range(2)]
        raw_in = [sem(f"raw_in{k}") for k in range(NS)]
        dense_cols_in = sem("dense_cols_in")
        dense_in = [sem(f"dense_in{i}") for i in range(JT)]
        w_dense_in = sem("w_dense_in")
        w_in = sem("w_in")
        w1_ready = sem("w1_ready")
        ident_zero = sem("ident_zero")
        ident_ready = sem("ident_ready")
        row_no_made = sem("row_no_made")
        row_no_ready = sem("row_no_ready")
        pads_ready = sem("pads_ready")
        hi_ready = sem("hi_ready")
        lo_ready = sem("lo_ready")
        onehot_ready = sem("onehot_ready")
        turn_full = sem("turn_full")
        turn_read = sem("turn_read")
        look_full = sem("look_full")
        look_read = sem("look_read")
        fixed_placed = sem("fixed_placed")
        prod_full = sem("prod_full")
        prod_read_v = sem("prod_read_v")
        prod_read_s = sem("prod_read_s")
        table_made = sem("table_made")
        table_wrapped = sem("table_wrapped")
        pairs_ready = sem("pairs_ready")
        pairs_turned = sem("pairs_turned")
        pairs_t_ready = sem("pairs_t_ready")
        l1_full = sem("l1_full")
        h1_ready = sem("h1_ready")
        l2_full = sem("l2_full")
        h2_ready = sem("h2_ready")
        l3_full = sem("l3_full")
        y_ready = sem("y_ready")
        y_stored = sem("y_stored")

        def feats_by_slot(i):
            return feats[i][:, :].rearrange("d (b w) -> d w b", w=W)

        block = ctx.enter_context(nc.Block())

        @block.sync
        def _(sp):
            def load_wanted(blk, k):
                v = NS * blk + k
                if not (isinstance(v, int) and v < 2):
                    sp.wait_ge(onehot_ready, v if k == 0 else v - 1)
                sp.dma_start(wanted[k % 2][:, :], small_ids[bass.ds(blk, 1), k, :].broadcast_to([CP, BS]))\
                    .then_inc(wanted_in[k % 2], 16)

            def store_result(t, j):
                sp.wait_ge(y_ready, t + 1)
                sp.dma_start(y[bass.ds(t, 1), :], y_sb[:, (j % 2) * P:(j % 2 + 1) * P]).then_inc(y_stored, 16)

            def load_table(k):
                sp.dma_start(fixed[0:CP, 1 + k, :], small_tables[k].rearrange("(p c) d -> p (c d)", c=CH))\
                    .then_inc(raw_in[k], 16)

            load_wanted(0, 0)
            load_table(0)
            load_wanted(0, 1)
            load_table(1)
            sp.dma_start(ids[1][:, :], gather_ids[1]).then_inc(ids_in[1], 16)
            load_table(2)
            load_table(3)
            for k in range(2, NS):
                load_wanted(0, k)
                if k + 2 < NS:
                    load_table(k + 2)
            load_wanted(1, 0)
            load_wanted(1, 1)

            def step_loads(b, j, more):
                if j < JT - 1:
                    for k in range(2 * j + 2, min(2 * j + 4, NS)):
                        load_wanted(b + 1, k)
                elif more:
                    load_wanted(b + 2, 0)
                    load_wanted(b + 2, 1)
                sp.wait_ge(gathered[j % 2], 16 * NG * (2 * b + j // 2 + 1))
                sp.dma_start(ids[j][:, :], gather_ids[bass.ds(JT * b + JT + j, 1)]
                             .rearrange("a p n -> (a p) n")).then_inc(ids_in[j], 16)
                sp.wait_ge(l1_full, JT * b + j + 1)
                sp.dma_start(dense[j][:, :], dense_rows[bass.ds(JT * b + JT + j, 1)]
                             .rearrange("a p n -> (a p) n")).then_inc(dense_in[j], 16)
                store_result(JT * b + j, j)

            def block_loads(b, more):
                sp.wait_ge(dense_cols_in, 16 * b + 16)
                sp.dma_start(fixed[:, 0, bass.ds(BS * ((b + 1) % 2), BS)], dense_cols[bass.ds(b + 1, 1)]
                             .rearrange("a p n -> (a p) n")).then_inc(dense_cols_in, 16)
                for j in range(JT):
                    step_loads(b, j, more)

            with sp.Fori(0, BLOCKS - 2) as b:
                block_loads(b, True)
            block_loads(BLOCKS - 2, False)
            for j in range(JT):
                store_result(JT * (BLOCKS - 1) + j, j)
            sp.wait_ge(y_stored, 16 * TILES)

        @block.gpsimd
        def _(gp):
            gp.iota(row_no_i[:, :], pattern=[[1, CH]], base=0, channel_multiplier=CH).then_inc(row_no_made, 1)
            gp.memset(ident[:, :], 0.0).then_inc(ident_zero, 1)

            def gather(j, ids_use):
                gp.wait_ge(ids_in[j], 16 * ids_use)
                gp.sem_inc(gather_begun, 1)
                for g in range(NG):
                    gp.indirect_dma_start(rows[j % 2][:, g, :], None, large_tables[g],
                                          bass.IndirectOffsetOnAxis(ap=ids[j][:, g:g + 1], axis=0))\
                        .then_inc(gathered[j % 2], 16)

            gather(0, 1)
            gp.wait_ge(ident_zero, 1)
            gp.affine_select(out=ident[:, :], in_=ident[:, :], compare_op=ALU.not_equal, fill=1.0,
                             base=0, pattern=[[-1, P]], channel_multiplier=1).then_inc(ident_ready, 1)
            gather(1, 1)

            def refill(b, i):
                gp.wait_ge(turn_full, START_USES + BLOCK_USES * b + (uses(i - 1) + NT if i else -1))
                gather((2 + i) % JT, b + 1 + (2 + i) // JT)

            with gp.Fori(0, BLOCKS - 1) as b:
                for i in range(JT):
                    refill(b, i)
            for i in range(2):
                refill(BLOCKS - 1, i)

        @block.scalar
        def _(act):
            def empty_features(i, banks, base):
                for n, (g, m) in enumerate(TURNS):
                    act.wait_ge(turn_full, base + n + 1)
                    nc.scalar.activation(feats_by_slot(i)[:, FIXED + g:FIXED + g + m, :],
                                         turn[(banks + n) % 2][:, 0:m * P].rearrange("d (f b) -> d f b", f=m),
                                         ACT.Copy).then_inc(turn_read, 1)

            def empty_even(k, half, bank, base):
                act.wait_ge(turn_full, base + 1)
                nc.scalar.activation(fixed[:, 1 + k, bass.ds(BS * half, BS)], turn[bank % 2][:, :], ACT.Copy)\
                    .then_inc(turn_read, 1)

            def empty_odd(k, half, full):
                act.wait_ge(look_full, full)
                nc.scalar.activation(fixed[:, 1 + k, bass.ds(BS * half, BS)], mlp_b[:, :], ACT.Copy)\
                    .then_inc(look_read, 1)

            def read_products(tile, i):
                act.wait_ge(prod_full, BUFS * tile + i + 1)
                for s in (2, 3):
                    last = nc.scalar.activation(diag_part(diag, s, i), prod_part(prod[i % 2], s), ACT.Copy)
                last.then_inc(prod_read_s, 1)

            act.dma_start(ids[0][:, :], gather_ids[0]).then_inc(ids_in[0], 16)
            act.dma_start(fixed[:, 0, 0:BS], dense_cols[0]).then_inc(dense_cols_in, 16)
            for j in range(2, JT):
                act.dma_start(ids[j][:, :], gather_ids[j]).then_inc(ids_in[j], 16)

            def empty_first(k):
                if k % 2:
                    empty_odd(k, 0, k // 2 + 1)
                elif k < NS - 1:
                    empty_even(k, 0, k // 2 + 1, k // 2)
                else:
                    empty_even(k, 0, START_USES, START_USES - 1)

            for k in range(NS):
                act.wait_ge(raw_in[k], 16)
                nc.scalar.activation(table_hi[:, k, :], fixed[0:CP, 1 + k, :], ACT.Copy).then_inc(hi_ready, 1)
                if k == 2:
                    act.dma_start(w1_sb[0:PR, 0:PC * H1].rearrange("p (c n) -> p c n", c=PC),
                                  w_pairs.rearrange("c p n -> p c n")).then_inc(w_in, 16)
                    act.dma_start(w1_sb[:, PC * H1:], w_dense).then_inc(w_dense_in, 16)
                    act.dma_start(table[:, 0:H1], w_dense2).then_inc(w_dense_in, 16)
                    act.dma_start(w2_sb[:, :].rearrange("p (c n) -> p c n", c=N1),
                                  w2.rearrange("(c p) n -> p c n", c=N1)).then_inc(w_in, 16)
                    act.dma_start(w3_sb[:, :], w3).then_inc(w_in, 16)
                    act.dma_start(b1_sb[:, :], b1).then_inc(w_in, 16)
                    act.dma_start(b2_sb[:, :], b2).then_inc(w_in, 16)
                    for j in range(JT):
                        act.dma_start(dense[j][:, :], dense_rows[j]).then_inc(dense_in[j], 16)
                if k:
                    empty_first(k - 1)
            act.wait_ge(pads_ready, 2)
            empty_features(0, EVEN, START_USES - 1 - NT)
            empty_first(NS - 1)
            for i in range(BUFS):
                read_products(0, i)
            act.wait_ge(w_in, 5 * 16)

            def step(b, j, look_up, front):
                base = START_USES + BLOCK_USES * b + uses(j, look_up)
                bank = uses(j, look_up)
                t = JT * b + j
                if front:
                    empty_features((j + 1) % 2, bank, base)
                if look_up and j:
                    empty_odd(2 * j - 1, (b + 1) % 2, ODD * (b + 1) + j)
                act.wait_ge(pairs_turned, t + 1)
                nc.scalar.activation(pairs_t[:, :], mlp_a[0:PR, 0:PC * P], ACT.Copy).then_inc(pairs_t_ready, 1)
                if look_up and j:
                    empty_even(2 * j, (b + 1) % 2, bank + NT, base + NT)
                act.wait_ge(l1_full, t + 1)
                for n in range(N1):
                    last = nc.scalar.activation(h1[:, n * P:(n + 1) * P], mlp_b[:, n * P:(n + 1) * P], ACT.Relu,
                                                bias=b1_sb[:, n:n + 1])
                last.then_inc(h1_ready, 1)
                if look_up and not j:
                    empty_even(0, (b + 1) % 2, bank + NT, base + NT)
                if front:
                    read_products(t + 1, 0)
                    read_products(t + 1, 1)
                act.wait_ge(l2_full, t + 1)
                for n in range(N2):
                    last = nc.scalar.activation(h2[:, n * P:(n + 1) * P], mlp_a[:, n * P:(n + 1) * P], ACT.Relu,
                                                bias=b2_sb[:, n:n + 1])
                last.then_inc(h2_ready, 1)
                if front:
                    read_products(t + 1, 2)
                    read_products(t + 1, 3)

            with act.Fori(0, BLOCKS - 1) as b:
                for j in range(JT):
                    step(b, j, True, True)
            for j in range(JT):
                step(BLOCKS - 1, j, False, j < JT - 1)

        @block.vector
        def _(dve):
            def one_hot(k, cs, use):
                if cs[0] == 0:
                    dve.wait_ge(wanted_in[k % 2], 16 * use)
                for c in cs:
                    made = nc.vector.tensor_scalar(onehot[k % 2][:, c, :], wanted[k % 2][:, :], row_no[:, c:c + 1],
                                                   None, ALU.is_equal)
                if cs[-1] == CH - 1:
                    made.then_inc(onehot_ready, 1)

            def place_fixed(i, j, half):
                nc.vector.tensor_copy(feats_by_slot(i)[:, 0:FIXED, :],
                                      fixed[:, :, bass.ds(BS * half + j * P, P)]).then_inc(fixed_placed, 1)

            def read_products(tile, i):
                dve.wait_ge(prod_full, BUFS * tile + i + 1)
                for s in (0, 1):
                    last = nc.vector.tensor_copy(diag_part(diag, s, i), prod_part(prod[i % 2], s))
                last.then_inc(prod_read_v, 1)

            def make_pairs(tile):
                dve.wait_ge(prod_read_v, BUFS * (tile + 1))
                dve.wait_ge(prod_read_s, BUFS * (tile + 1))
                nc.vector.transpose(table[:, :].rearrange("p (f g) -> p g f", g=XW)[:, 0:SLOTS, :],
                                    diag[:, :].rearrange("p (g n) -> p g n", n=GROUPS)).then_inc(table_made, 1)
                dve.wait_ge(table_made, tile + 1)
                rows_of = table[:, :].rearrange("p (f g) -> p f g", g=XW)[:, SLOTS - DELTAS:SLOTS, :]
                nc.vector.tensor_copy(rows_of[:, :, SLOTS:XW], rows_of[:, :, 0:DELTAS]).then_inc(table_wrapped, 1)
                dve.wait_ge(table_wrapped, tile + 1)
                if not (isinstance(tile, int) and tile == 0):
                    dve.wait_ge(pairs_turned, tile)
                nc.vector.tensor_copy(pairs[:, :].rearrange("p (f k) -> p f k", k=DELTAS),
                                      table[:, 1:1 + SLOTS * (XW + 1)]
                                      .rearrange("p (f g) -> p f g", g=XW + 1)[:, :, 0:DELTAS])\
                    .then_inc(pairs_ready, 1)

            dve.wait_ge(row_no_made, 1)
            nc.vector.tensor_copy(row_no[:, :], row_no_i[:, :]).then_inc(row_no_ready, 1)
            dve.wait_ge(row_no_ready, 1)
            for k in range(NS):
                if k >= 2:
                    if k % 2:
                        dve.wait_ge(look_full, k // 2)
                    else:
                        dve.wait_ge(turn_full, k // 2)
                one_hot(k, range(CH), k // 2 + 1)
                dve.wait_ge(hi_ready, k + 1)
                nc.vector.tensor_tensor(table_lo[:, k, :], fixed[0:CP, 1 + k, :],
                                        table_hi[:, k, :].bitcast(F32), ALU.subtract).then_inc(lo_ready, 1)
                if k == 0:
                    for i in range(2):
                        nc.vector.memset(feats[i][:, :].rearrange("d (b w) -> d b w", w=W)[:, :, SLOTS:W], 0.0)\
                            .then_inc(pads_ready, 1)
            dve.wait_ge(w_dense_in, 32)
            nc.vector.tensor_tensor(w1_sb[:, PC * H1:], w1_sb[:, PC * H1:], table[:, 0:H1], ALU.add)\
                .then_inc(w1_ready, 1)
            dve.wait_ge(turn_read, START_USES)
            dve.wait_ge(look_read, ODD)
            dve.wait_ge(dense_cols_in, 16)
            place_fixed(0, 0, 0)
            for i in range(BUFS):
                read_products(0, i)
            make_pairs(0)

            def copy_result(t, j):
                dve.wait_ge(l3_full, t + 1)
                if j:
                    dve.wait_ge(y_stored, 16 * t)
                nc.vector.tensor_copy(y_sb[:, (j % 2) * P:(j % 2 + 1) * P], mlp_a[0:1, N2 * P:(N2 + 1) * P])\
                    .then_inc(y_ready, 1)

            def step(b, j, look_up, front):
                base = START_USES + BLOCK_USES * b
                t = JT * b + j
                even, odd = EVEN * (b + 1), ODD * (b + 1)
                if front:
                    if j == JT - 1:
                        dve.wait_ge(turn_read, base + BLOCK_USES)
                        dve.wait_ge(look_read, ODD * (b + 2))
                        dve.wait_ge(dense_cols_in, 16 * (b + 2))
                    place_fixed((j + 1) % 2, (j + 1) % JT, b % 2 if j < JT - 1 else (b + 1) % 2)
                makes = look_up and j < JT - 1
                if look_up and j == 0:
                    dve.wait_ge(turn_full, base)
                    one_hot(0, range(CH), even + 1)
                if makes:
                    dve.wait_ge(look_full, odd + j)
                    one_hot(2 * j + 1, range(CH), odd + j + 1)
                for i in range(BUFS):
                    if front:
                        read_products(t + 1, i)
                    if makes:
                        if i == 0:
                            dve.wait_ge(turn_full, base + uses(j + 1))
                        one_hot(2 * j + 2, range(2 * i, 2 * i + 2), even + j + 2)
                copy_result(t, j)
                if front:
                    make_pairs(t + 1)

            with dve.Fori(0, BLOCKS - 1) as b:
                for j in range(JT):
                    step(b, j, True, True)
            for j in range(JT):
                step(BLOCKS - 1, j, False, j < JT - 1)

        @block.tensor
        def _(pe):
            def turn_bank(bank, filled):
                if not (isinstance(filled, int) and filled < 2):
                    pe.wait_ge(turn_read, filled - 1)
                return turn[bank % 2]

            def look_up_part(k, bank, chunks):
                for c in chunks:
                    for part in (table_hi, table_lo):
                        last = nc.tensor.matmul(bank[:, :], part[:, k, c * D:(c + 1) * D], onehot[k % 2][:, c, :],
                                                start=(c == 0 and part is table_hi),
                                                stop=(c == CH - 1 and part is table_lo))
                return last

            def look_up_even(k, ready, bank, filled):
                bank = turn_bank(bank, filled)
                pe.wait_ge(onehot_ready, ready)
                look_up_part(k, bank, range(CH)).then_inc(turn_full, 1)

            def turn_features(i, arrivals, bank, filled, odd=None, ready=0):
                pe.wait_ge(gathered[i], 16 * NG * arrivals)
                for n, (g, m) in enumerate(TURNS):
                    to = turn_bank(bank + n, filled + n)
                    for f in range(m):
                        last = nc.tensor.transpose(to[:, f * P:(f + 1) * P], rows[i][:, g + f, :], ident[:, :])
                    last.then_inc(turn_full, 1)
                    if odd is not None and n < NT - 1:
                        if n == 0:
                            pe.wait_ge(onehot_ready, ready)
                        looked = look_up_part(odd, mlp_b, range(2 * n, 2 * n + 2))
                        if n == NT - 2:
                            looked.then_inc(look_full, 1)

            def products(tile, parity, i):
                n = BUFS * tile + i
                if not (isinstance(n, int) and n < 2):
                    pe.wait_ge(prod_read_v, n - 1)
                    pe.wait_ge(prod_read_s, n - 1)
                x = feats[parity]
                for g in range(BUF_GROUPS):
                    own = x[:, (i * BUF_GROUPS + g) * P:(i * BUF_GROUPS + g + 1) * P]
                    at = (g // GB) * BANK + (g % GB) * GS * SLOTS
                    last = nc.tensor.matmul(prod[i % 2][:, at:at + GS * SLOTS], own,
                                            own.rearrange("d (s w) -> d s w", w=W)[:, :, 0:SLOTS],
                                            start=True, stop=True)
                last.then_inc(prod_full, 1)

            for k in range(NS):
                if k == NS - 1:
                    pe.wait_ge(ident_ready, 1)
                    turn_features(0, 1, EVEN, EVEN - 1)
                pe.wait_ge(lo_ready, k + 1)
                if k % 2:
                    if k > 1:
                        pe.wait_ge(look_read, k // 2)
                    pe.wait_ge(onehot_ready, k + 1)
                    look_up_part(k, mlp_b, range(CH)).then_inc(look_full, 1)
                elif k < NS - 1:
                    look_up_even(k, k + 1, k // 2 + 1, k // 2)
                else:
                    look_up_even(k, k + 1, START_USES, START_USES - 1)
            pe.wait_ge(turn_read, START_USES)
            pe.wait_ge(fixed_placed, 1)
            for i in range(BUFS):
                products(0, 0, i)
            pe.wait_ge(w1_ready, 1)
            pe.wait_ge(w_in, 5 * 16)

            def step(b, j, look_up, front):
                base = START_USES + BLOCK_USES * b + uses(j, look_up)
                bank = uses(j, look_up)
                t = JT * b + j
                if front:
                    odd = 2 * j - 1 if look_up and j else None
                    turn_features((j + 1) % 2, 2 * b + (j + 1) // 2 + 1, bank, base, odd, NS * (b + 1) + 2 * j)
                pe.wait_ge(pairs_ready, t + 1)
                for c in range(PC):
                    last = nc.tensor.transpose(mlp_a[0:PR, c * P:(c + 1) * P], pairs[:, c * PR:(c + 1) * PR],
                                               ident[:, :])
                last.then_inc(pairs_turned, 1)
                if look_up and j:
                    look_up_even(2 * j, NS * (b + 1) + 2 * j + 1, bank + NT, base + NT)
                pe.wait_ge(pairs_t_ready, t + 1)
                pe.wait_ge(dense_in[j], 16 * (b + 1))
                if look_up and j:
                    pe.wait_ge(look_read, ODD * (b + 1) + j)
                for n in range(N1):
                    for c in range(PC):
                        nc.tensor.matmul(mlp_b[:, n * P:(n + 1) * P], w1_sb[0:PR, c * H1 + n * P:c * H1 + (n + 1) * P],
                                         pairs_t[:, c * P:(c + 1) * P], start=(c == 0), stop=False)
                    last = nc.tensor.matmul(mlp_b[:, n * P:(n + 1) * P],
                                            w1_sb[:, PC * H1 + n * P:PC * H1 + (n + 1) * P],
                                            dense[j][:, :], start=False, stop=True)
                last.then_inc(l1_full, 1)
                if look_up and not j:
                    look_up_even(0, NS * (b + 1) + 1, bank + NT, base + NT)
                if front:
                    pe.wait_ge(turn_read, base + NT)
                    pe.wait_ge(fixed_placed, t + 2)
                    products(t + 1, (j + 1) % 2, 0)
                    products(t + 1, (j + 1) % 2, 1)
                pe.wait_ge(h1_ready, t + 1)
                for n in range(N2):
                    for c in range(N1):
                        last = nc.tensor.matmul(mlp_a[:, n * P:(n + 1) * P],
                                                w2_sb[:, c * H2 + n * P:c * H2 + (n + 1) * P],
                                                h1[:, c * P:(c + 1) * P], start=(c == 0), stop=(c == N1 - 1))
                last.then_inc(l2_full, 1)
                if front:
                    products(t + 1, (j + 1) % 2, 2)
                    products(t + 1, (j + 1) % 2, 3)
                pe.wait_ge(h2_ready, t + 1)
                for c in range(N2):
                    last = nc.tensor.matmul(mlp_a[0:1, N2 * P:(N2 + 1) * P], w3_sb[:, c:c + 1],
                                            h2[:, c * P:(c + 1) * P], start=(c == 0), stop=(c == N2 - 1))
                last.then_inc(l3_full, 1)

            with pe.Fori(0, BLOCKS - 1) as b:
                for j in range(JT):
                    step(b, j, True, True)
            for j in range(JT):
                step(BLOCKS - 1, j, False, j < JT - 1)


def prod_part(buf, s):
    return buf[W * s:W * (s + 1), :].rearrange("p (k r) -> p k r", k=BUF_BANKS)[:, :, 0:GB * GS * SLOTS]\
        .rearrange("p k (g r) -> p k g r", g=GB)[:, :, :, s * SLOTS:(s + 1) * SLOTS]


def diag_part(diag, s, i):
    return diag[W * s:W * (s + 1), :].rearrange("p (f n) -> p n f", n=GROUPS)[
        :, i * BUF_GROUPS:(i + 1) * BUF_GROUPS, :].rearrange("p (k g) f -> p k g f", k=BUF_BANKS)


def kernel(**inputs):
    import concourse.bacc as bacc
    from concourse import mybir as _mybir
    from concourse.bass_utils import run_bass_kernel_spmd

    arr = {k: np.ascontiguousarray(v) for k, v in inputs.items()}
    ids, x, w1 = arr["ids"], arr["r_dense_features"], arr["W_top1"]

    by_column = ids.reshape(TILES, GS, GROUPS, N_TABLES).transpose(0, 2, 1, 3).reshape(TILES, P, N_TABLES)
    x_column = x.reshape(TILES, GS, GROUPS, D).transpose(0, 2, 1, 3).reshape(BLOCKS, BS, D)
    first = np.arange(SLOTS).repeat(DELTAS)
    second = (first + np.tile(np.arange(1, DELTAS + 1), SLOTS)) % SLOTS
    a, c = np.array(ORDER)[first], np.array(ORDER)[second]
    lo, hi = np.minimum(a, c), np.maximum(a, c)
    pair_row = D + lo * SLOTS - lo * (lo + 1) // 2 + hi - lo - 1

    feeds = {
        "gather_ids": by_column[:, :, list(LARGE)],
        "small_ids": by_column.reshape(BLOCKS, BS, N_TABLES)[:, :, list(SMALL)].transpose(0, 2, 1),
        "dense_cols": x_column.transpose(0, 2, 1),
        "dense_rows": x.reshape(TILES, P, D).transpose(0, 2, 1),
        **{f"tbl_{f}": arr[f"tbl_{f}"] for f in range(N_TABLES)},
        "w_pairs": w1[pair_row].reshape(PC, PR, H1),
        "w_dense": w1[:D],
        "w_dense2": w1[D + PAIRS:],
        "w2": arr["W_top2"],
        "w3": arr["W_top3"].reshape(N2, P).T,
        "b1": arr["b_top1"].reshape(N1, P).T,
        "b2": arr["b_top2"].reshape(N2, P).T,
    }
    feeds = {f"in_{k}": np.ascontiguousarray(v) for k, v in feeds.items()}
    nc = bacc.Bacc("TRN2", target_bir_lowering=False, num_devices=1)
    ap = {k: nc.dram_tensor(k, v.shape, _mybir.dt.from_np(v.dtype), kind="ExternalInput").ap()
          for k, v in feeds.items()}
    y = nc.dram_tensor("out_y", (TILES, P), F32, kind="ExternalOutput").ap()
    tower_program(nc, ap["in_gather_ids"], ap["in_small_ids"], ap["in_dense_cols"], ap["in_dense_rows"],
                  [ap[f"in_tbl_{f}"] for f in SMALL], [ap[f"in_tbl_{f}"] for f in LARGE],
                  ap["in_w_pairs"], ap["in_w_dense"], ap["in_w_dense2"], ap["in_w2"], ap["in_w3"],
                  ap["in_b1"], ap["in_b2"], y)
    r = run_bass_kernel_spmd(nc, [feeds], core_ids=[0])
    return r.results[0]["out_y"].reshape(BATCH, 1)
```
